# Optimizing a Trainium2 kernel written in Bass

```python
import numpy as np
import jax
import jax.numpy as jnp

def _softmax(x, axis=-1):
    return jax.nn.softmax(x, axis=axis)

def _gelu(x):
    return jax.nn.gelu(x, approximate=True)

def _silu(x):
    return jax.nn.silu(x)

def _sigmoid(x):
    return jax.nn.sigmoid(x)

def _layernorm(x, axis=-1, eps=1e-05):
    m = jnp.mean(x, axis=axis, keepdims=True)
    v = jnp.var(x, axis=axis, keepdims=True)
    return (x - m) / jnp.sqrt(v + eps)

def _scatter_add(tgt, idx, src, axis=0):
    return tgt.at[idx].add(src)

def _segment_sum(src, seg, n):
    return jax.ops.segment_sum(src, seg, n)
kernel_name = 'mk_cond_resid_d4_seqx_r8_59fc8a'

def setup_inputs(seed: int=0):
    np.random.seed(seed)
    _w = jnp.asarray

    def _rec_inputs():
        import jax
        import jax.numpy as jnp
        _rk = jax.random.key(seed)
        x = -0.0002071 + 1 * jax.random.normal(jax.random.fold_in(_rk, 1), (2, 512, 128), jnp.float32)
        _lenS = 512 - jax.random.randint(jax.random.fold_in(_rk, 7), (2,), 0, max(1, 512 // 4) + 1, jnp.int32)
        _lenS2 = 512 - jax.random.randint(jax.random.fold_in(_rk, 8), (2,), 0, max(1, 512 // 4) + 1, jnp.int32)
        cond_8 = jax.random.uniform(jax.random.fold_in(_rk, 11), (2, 8), jnp.float32, 0.0, 0.983423)
        return (x, cond_8)
    x, cond_8 = _rec_inputs()

    def _L0_cond_setup():
        import jax, jax.numpy as jnp
        import numpy as np
        R = 16
        ALPHA = 32.0
        SCALING = ALPHA / R
        key = jax.random.key(seed)
        ks = jax.random.split(key, 6)
        B, T, C, O, E = (16, 1500, 128, 128, 8)
        x = jax.random.normal(ks[0], (B, T, C), dtype=jnp.float32)
        w = jax.random.uniform(ks[1], (B, E), dtype=jnp.float32)
        W_base = jax.random.normal(ks[2], (O, C), dtype=jnp.float32) * 0.02
        b_base = jax.random.normal(ks[3], (O,), dtype=jnp.float32) * 0.02
        As = jax.random.normal(ks[4], (E, R, C), dtype=jnp.float32) * 0.02
        Bs = jax.random.normal(ks[5], (E, O, R), dtype=jnp.float32) * 0.02
        return {'x': x, 'w': w, 'W_base': W_base, 'b_base': b_base, 'As': As, 'Bs': Bs}
    _L0_cond_all = _L0_cond_setup()
    _L0_cond_in = {k: v for k, v in _L0_cond_all.items() if k in ('W_base', 'b_base', 'As', 'Bs')}
    del _L0_cond_all

    def _L1_cond_setup():
        import jax, jax.numpy as jnp
        import numpy as np
        TOP_K = 2
        NUM_MOE_LAYERS = 12

        def _gemma_mlp(x, gate_w, up_w, down_w):
            g = jnp.einsum('bsh,hi->bsi', x, gate_w)
            u = jnp.einsum('bsh,hi->bsi', x, up_w)
            return jnp.einsum('bsi,ih->bsh', jax.nn.gelu(g, approximate=True) * u, down_w)
        key = jax.random.key(seed)
        ks = jax.random.split(key, 8)
        B, S, H, I, E = (32, 32, 128, 512, 8)
        std = 0.02
        return {'x': jax.random.normal(ks[0], (B, S, H), jnp.float32), 'router_logits': jax.random.normal(ks[1], (B, E), jnp.float32), 'skill_gate': jax.random.normal(ks[2], (E, H, I), jnp.float32) * std, 'skill_up': jax.random.normal(ks[3], (E, H, I), jnp.float32) * std, 'skill_down': jax.random.normal(ks[4], (E, I, H), jnp.float32) * std, 'shared_gate': jax.random.normal(ks[5], (H, I), jnp.float32) * std, 'shared_up': jax.random.normal(ks[6], (H, I), jnp.float32) * std, 'shared_down': jax.random.normal(ks[7], (I, H), jnp.float32) * std}
    _L1_cond_all = _L1_cond_setup()
    _L1_cond_in = {k: v for k, v in _L1_cond_all.items() if k in ('skill_gate', 'skill_up', 'skill_down', 'shared_gate', 'shared_up', 'shared_down')}
    del _L1_cond_all

    def _L2_cond_setup():
        import jax, jax.numpy as jnp
        import numpy as np
        key = jax.random.key(seed)
        k1, k2, k3, k4, k5 = jax.random.split(key, 5)
        B, N, T, O, G = (32, 32, 128, 128, 8)
        x = jax.random.normal(k1, (B, N, T), dtype=jnp.float32)
        y = jax.random.uniform(k2, (B, G), dtype=jnp.float32)
        weight = jax.random.normal(k3, (G, O, T), dtype=jnp.float32) * (1.0 / np.sqrt(T))
        mask = jax.random.uniform(k4, (O, T), dtype=jnp.float32)
        bias = jax.random.normal(k5, (O,), dtype=jnp.float32)
        return {'x': x, 'y': y, 'weight': weight, 'mask': mask, 'bias': bias}
    _L2_cond_all = _L2_cond_setup()
    _L2_cond_in = {k: v for k, v in _L2_cond_all.items() if k in ('weight', 'mask', 'bias')}
    del _L2_cond_all

    def _L3_cond_setup():
        import jax, jax.numpy as jnp
        import numpy as np
        key = jax.random.key(seed)
        k1, k2, k3, k4, k5 = jax.random.split(key, 5)
        B, N, T, O, G = (32, 32, 128, 128, 8)
        x = jax.random.normal(k1, (B, N, T), dtype=jnp.float32)
        y = jax.random.uniform(k2, (B, G), dtype=jnp.float32)
        weight = jax.random.normal(k3, (G, O, T), dtype=jnp.float32) * (1.0 / np.sqrt(T))
        mask = jax.random.uniform(k4, (O, T), dtype=jnp.float32)
        bias = jax.random.normal(k5, (O,), dtype=jnp.float32)
        return {'x': x, 'y': y, 'weight': weight, 'mask': mask, 'bias': bias}
    _L3_cond_all = _L3_cond_setup()
    _L3_cond_in = {k: v for k, v in _L3_cond_all.items() if k in ('weight', 'mask', 'bias')}
    del _L3_cond_all
    return {'x': x, 'cond_8': cond_8, 'L0_cond_W_base': _L0_cond_in['W_base'], 'L0_cond_b_base': _L0_cond_in['b_base'], 'L0_cond_As': _L0_cond_in['As'], 'L0_cond_Bs': _L0_cond_in['Bs'], 'L1_cond_skill_gate': _L1_cond_in['skill_gate'], 'L1_cond_skill_up': _L1_cond_in['skill_up'], 'L1_cond_skill_down': _L1_cond_in['skill_down'], 'L1_cond_shared_gate': _L1_cond_in['shared_gate'], 'L1_cond_shared_up': _L1_cond_in['shared_up'], 'L1_cond_shared_down': _L1_cond_in['shared_down'], 'L2_cond_weight': _L2_cond_in['weight'], 'L2_cond_mask': _L2_cond_in['mask'], 'L2_cond_bias': _L2_cond_in['bias'], 'L3_cond_weight': _L3_cond_in['weight'], 'L3_cond_mask': _L3_cond_in['mask'], 'L3_cond_bias': _L3_cond_in['bias']}

def reference(x, cond_8, L0_cond_W_base, L0_cond_b_base, L0_cond_As, L0_cond_Bs, L1_cond_skill_gate, L1_cond_skill_up, L1_cond_skill_down, L1_cond_shared_gate, L1_cond_shared_up, L1_cond_shared_down, L2_cond_weight, L2_cond_mask, L2_cond_bias, L3_cond_weight, L3_cond_mask, L3_cond_bias):
    import jax
    import jax.numpy as jnp

    def _L0_cond_ref(x, w, W_base, b_base, As, Bs):
        import jax, jax.numpy as jnp
        import numpy as np
        R = 16
        ALPHA = 32.0
        SCALING = ALPHA / R
        out = jnp.einsum('btc,oc->bto', x, W_base) + b_base
        h = jnp.einsum('btc,erc->bter', x, As)
        lora = jnp.einsum('bter,eor,be->bto', h, Bs, w)
        return out + lora * SCALING

    def _L1_cond_ref(x, router_logits, skill_gate, skill_up, skill_down, shared_gate, shared_up, shared_down):
        import jax, jax.numpy as jnp
        import numpy as np
        TOP_K = 2
        NUM_MOE_LAYERS = 12

        def _gemma_mlp(x, gate_w, up_w, down_w):
            g = jnp.einsum('bsh,hi->bsi', x, gate_w)
            u = jnp.einsum('bsh,hi->bsi', x, up_w)
            return jnp.einsum('bsi,ih->bsh', jax.nn.gelu(g, approximate=True) * u, down_w)
        B = x.shape[0]
        E = skill_gate.shape[0]
        rw = jax.nn.softmax(router_logits.astype(jnp.float32), axis=-1)
        w, sel = jax.lax.top_k(rw, TOP_K)
        w = w / w.sum(axis=-1, keepdims=True)
        w = w.astype(x.dtype)
        scale = 1.0 / NUM_MOE_LAYERS
        w = scale * w + (1.0 - scale) * jax.lax.stop_gradient(w)
        dense_w = jnp.zeros((B, E), x.dtype).at[jnp.arange(B)[:, None], sel].add(w)

        def step(acc, params):
            g, u, d, we = params
            return (acc + we[:, None, None] * _gemma_mlp(x, g, u, d), None)
        out, _ = jax.lax.scan(step, jnp.zeros_like(x), (skill_gate, skill_up, skill_down, dense_w.T))
        out = out + _gemma_mlp(x, shared_gate, shared_up, shared_down)
        return out

    def _L2_cond_ref(x, y, weight, mask, bias):
        import jax, jax.numpy as jnp
        import numpy as np
        masked_w = weight * mask[None, :, :]
        w_bot = jnp.einsum('bg,got->bot', y, masked_w)
        return jnp.einsum('bnt,bot->bno', x, w_bot) + bias

    def _L3_cond_ref(x, y, weight, mask, bias):
        import jax, jax.numpy as jnp
        import numpy as np
        masked_w = weight * mask[None, :, :]
        w_bot = jnp.einsum('bg,got->bot', y, masked_w)
        return jnp.einsum('bnt,bot->bno', x, w_bot) + bias
    x = x + _L0_cond_ref(x, cond_8, L0_cond_W_base, L0_cond_b_base, L0_cond_As, L0_cond_Bs)
    x = x + _L1_cond_ref(x, cond_8, L1_cond_skill_gate, L1_cond_skill_up, L1_cond_skill_down, L1_cond_shared_gate, L1_cond_shared_up, L1_cond_shared_down)
    x = x + _L2_cond_ref(x, cond_8, L2_cond_weight, L2_cond_mask, L2_cond_bias)
    x = x + _L3_cond_ref(x, cond_8, L3_cond_weight, L3_cond_mask, L3_cond_bias)
    return x

_drawn_inputs = setup_inputs


def setup_inputs(seed=0):
    import zlib

    import numpy as np

    out = dict(_drawn_inputs(seed))
    spreads = {}
    factors = {'L0_cond_b_base': 3.951,
     'L1_cond_skill_gate': 8.0,
     'L1_cond_skill_up': 8.0,
     'L1_cond_skill_down': 8.0,
     'L1_cond_shared_gate': 6.409,
     'L1_cond_shared_up': 6.284,
     'L1_cond_shared_down': 6.285}
    for name, (base, spread) in spreads.items():
        noise = np.random.default_rng([zlib.crc32(name.encode()), seed]).standard_normal(out[name].shape)
        drawn = base * np.exp(spread * noise) if base else spread * noise
        out[name] = jnp.asarray(drawn.astype(out[name].dtype))
    for name, factor in factors.items():
        out[name] = (out[name] * factor).astype(out[name].dtype)
    return out
```

```python
from contextlib import ExitStack

import concourse.bass as bass
from concourse import mybir

ALU = mybir.AluOpType
ACT = mybir.ActivationFunctionType
AX_X = mybir.AxisListType.X
F32 = mybir.dt.float32
F32R = mybir.dt.float32r
U32 = mybir.dt.uint32

P = 128
LORA_SCALING = 32.0 / 16


def cond_resid_kernel(
    nc: bass.Bass,
    x: bass.AP,
    cond: bass.AP,
    w_base: bass.AP,
    b_base: bass.AP,
    lora_a: bass.AP,
    lora_b: bass.AP,
    skill_gate: bass.AP,
    skill_up: bass.AP,
    skill_down: bass.AP,
    shared_gate: bass.AP,
    shared_up: bass.AP,
    shared_down: bass.AP,
    w_l2: bass.AP,
    mask_l2: bass.AP,
    bias_l2: bass.AP,
    w_l3: bass.AP,
    mask_l3: bass.AP,
    bias_l3: bass.AP,
    out: bass.AP,
):
    B, T, D = x.shape
    E = cond.shape[1]
    R = lora_a.shape[1]
    I = skill_gate.shape[2]
    assert D == P and E * R == P and T == 4 * P and B == 2
    NT = T // P
    NC = I // P
    OL = P // E
    OH = P // OL

    UNITS = [(b, k) for b in range(B) for k in range(3)]
    STEPS = len(UNITS) * NC
    SLOTS = 3
    HALF = STEPS // B
    NSETS = 1 + 2 * B

    def weight_set(b, k):
        return 0 if k == 0 else 2 * b + k

    ctx = ExitStack()
    with ctx:

        def sb(name, shape, dt=F32):
            return ctx.enter_context(nc.sbuf_tensor(name, shape, dt))

        def sem(name):
            return ctx.enter_context(nc.semaphore(name))

        ident = sb("ident", [P, P])
        ones = sb("ones", [P, P])
        x_nat = sb("x_nat", [P, B, NT, D])
        xT = sb("xT", [P, B, T])
        a_sb = sb("a_sb", [P, D])
        b_nat = sb("b_nat", [P, E, R])
        wbase_sb = sb("wbase_sb", [P, D])
        wbase_i = sb("wbase_i", [P, D])
        bT_w = sb("bT_w", [P, B, P])
        w0_eff = sb("w0_eff", [P, B, P])
        bias0 = sb("bias0", [P, 1])
        cond_col = sb("cond_col", [P, B])
        cond_row = sb("cond_row", [P, B, E])
        own_group = sb("own_group", [P, 1, E])
        cond_own = sb("cond_own", [P, B, E])
        top_val = sb("top_val", [P, B, 8])
        top_idx = sb("top_idx", [P, B, 8], U32)
        top_dif = sb("top_dif", [P, B, 8])
        top_exp = sb("top_exp", [P, B, 8])
        z_sum = sb("z_sum", [P, B, 1])
        z_inv = sb("z_inv", [P, B, 1])
        probs = sb("probs", [P, B, 2])
        pair_sum = sb("pair_sum", [P, B, 1])
        pair_inv = sb("pair_inv", [P, B, 1])
        route_w = sb("route_w", [P, B, 2])

        x1 = sb("x1", [P, B, T])
        x1_hi = sb("x1_hi", [P, B, T], F32R)
        x1_lo = sb("x1_lo", [P, B, T], F32R)
        w_raw = sb("w_raw", [P, NSETS, 3, I])
        w_hi = sb("w_hi", [P, NSETS, 3, I], F32R)
        w_lo = sb("w_lo", [P, NSETS, 3, I], F32R)
        gelu_g = sb("gelu_g", [P, SLOTS, T])
        h = sb("h", [P, SLOTS, T])
        h_hi = sb("h_hi", [P, SLOTS, T], F32R)
        h_lo = sb("h_lo", [P, SLOTS, T], F32R)

        gw = sb("gw", [P, 2, OH, P])
        mask_nat = sb("mask_nat", [P, 2, P])
        maskT = sb("maskT", [P, 2, P])
        delta = sb("delta", [P, OL])
        ymat = sb("ymat", [P, B, OL])
        wsum = sb("wsum", [P, 2, B, P])
        wres = sb("wres", [P, 2, B, P])
        a2_nat = sb("a2_nat", [P, B, P])
        w23 = sb("w23", [P, B, P])
        bias2 = sb("bias2", [P, 1])
        bias2_b = sb("bias2_b", [P, P])
        bias3_b = sb("bias3_b", [P, P])
        bias23 = sb("bias23", [P, B, P])
        x2T = sb("x2T", [P, B, T])
        out_sb = sb("out_sb", [P, B, NT, D])

        def bank(name):
            return ctx.enter_context(nc.psum_tensor(name, [P, T], F32))

        gate_ps = [bank(f"gate_ps{i}") for i in range(SLOTS)]
        up_ps = [bank(f"up_ps{i}") for i in range(SLOTS)]
        acc_ps = [bank(f"acc_ps{b}") for b in range(B)]
        xT_ps = [gate_ps[0], up_ps[0]]
        bT_ps = gate_ps[1]
        w0_ps = up_ps[1]
        x1_ps = [gate_ps[2], up_ps[2]]
        fold_ps = acc_ps[1]
        tail_ps = [gate_ps[0], up_ps[0]]

        x_in = [sem(f"x_in{b}") for b in range(B)]
        condrow_in = sem("condrow_in")
        lora_a_in = sem("lora_a_in")
        lora_b_in = sem("lora_b_in")
        wbase_in = sem("wbase_in")
        bias0_in = sem("bias0_in")
        w_in = [[sem(f"w_in{s}_{m}") for m in range(3)] for s in range(NSETS)]
        gw_in = sem("gw_in")
        mask_in = sem("mask_in")
        bias23_in = sem("bias23_in")
        out_done = sem("out_done")

        ident_ready = sem("ident_ready")
        wbase_i_ready = sem("wbase_i_ready")
        xT_ps_ready = sem("xT_ps_ready")
        xT_ready = sem("xT_ready")
        bT_ps_ready = sem("bT_ps_ready")
        bT_w_ready = sem("bT_w_ready")
        w0_ps_ready = sem("w0_ps_ready")
        w0_ready = sem("w0_ready")
        x1_ps_ready = sem("x1_ps_ready")
        x1_hi_ready = sem("x1_hi_ready")
        x1_ready = sem("x1_ready")
        x1_lo_ready = sem("x1_lo_ready")
        topk_step = sem("topk_step")
        top_exp_ready = sem("top_exp_ready")
        route_step = sem("route_step")
        w_hi_ready = sem("w_hi_ready")
        w_lo_ready = sem("w_lo_ready")
        gate_ready = sem("gate_ready")
        up_ready = sem("up_ready")
        gelu_done = sem("gelu_done")
        h_ready = sem("h_ready")
        h_hi_ready = sem("h_hi_ready")
        h_lo_ready = sem("h_lo_ready")
        down_done = sem("down_done")
        mask_ps_ready = sem("mask_ps_ready")
        maskT_ready = sem("maskT_ready")
        select_step = sem("select_step")
        ymat_ready = sem("ymat_ready")
        wsum_ps_ready = sem("wsum_ps_ready")
        wsum_ready = sem("wsum_ready")
        wres_ready = sem("wres_ready")
        bias2_b_ready = sem("bias2_b_ready")
        a2_ps_ready = sem("a2_ps_ready")
        a2_ready = sem("a2_ready")
        w23_ps_ready = sem("w23_ps_ready")
        w23_ready = sem("w23_ready")
        x2_ready = sem("x2_ready")
        out_ps_ready = sem("out_ps_ready")
        out_ready = sem("out_ready")

        ROUTE_STEPS = 6

        block = ctx.enter_context(nc.Block())

        @block.sync
        def _(sp):
            x_v = x.rearrange("b (p n) d -> b p n d", n=NT)
            sp.dma_start(x_nat[:, 0], x_v[0]).then_inc(x_in[0], 16)
            sp.dma_start(cond_row[:].rearrange("p b e -> p (b e)"),
                         cond.rearrange("b e -> (b e)").partition_broadcast(P)).then_inc(condrow_in, 16)
            sp.dma_start(x_nat[:, 1], x_v[1]).then_inc(x_in[1], 16)
            sp.dma_start(w_raw[:, 0, 0], shared_gate).then_inc(w_in[0][0], 16)
            sp.dma_start(w_raw[:, 0, 1], shared_up).then_inc(w_in[0][1], 16)
            sp.dma_start(w_raw[:, 0, 2].rearrange("p (c d) -> p c d", c=NC),
                         shared_down.rearrange("(c p) d -> p c d", p=P)).then_inc(w_in[0][2], 16)

            def fetch_experts(b):
                for k in range(2):
                    e = sp.value_load(top_idx[0:1, b, k:k + 1], min_val=0, max_val=E - 1)
                    s = weight_set(b, k + 1)
                    sp.dma_start(w_raw[:, s, 0], skill_gate[bass.ds(e, 1)].rearrange("a h i -> (a h) i")) \
                        .then_inc(w_in[s][0], 16)
                    sp.dma_start(w_raw[:, s, 1], skill_up[bass.ds(e, 1)].rearrange("a h i -> (a h) i")) \
                        .then_inc(w_in[s][1], 16)
                    sp.dma_start(w_raw[:, s, 2].rearrange("p (c d) -> p c d", c=NC),
                                 skill_down[bass.ds(e, 1)].rearrange("a (c p) d -> p (a c) d", p=P)) \
                        .then_inc(w_in[s][2], 16)

            sp.wait_ge(topk_step, 2 * B)
            fetch_experts(0)
            for layer, (w, m) in enumerate([(w_l2, mask_l2), (w_l3, mask_l3)]):
                sp.dma_start(mask_nat[:, layer], m).then_inc(mask_in, 16)
                sp.dma_start(gw[:, layer], w.rearrange("g (ol oh) t -> (g ol) oh t", oh=OH)).then_inc(gw_in, 16)
            sp.dma_start(bias2[:], bias_l2.rearrange("(p a) -> p a", a=1)).then_inc(bias23_in, 16)
            sp.dma_start(bias3_b[:], bias_l3.partition_broadcast(P)).then_inc(bias23_in, 16)
            fetch_experts(1)

            out_v = out.rearrange("b (p n) d -> b p n d", n=NT)
            sp.wait_ge(out_ready, 1)
            sp.dma_start(out_v[0], out_sb[:, 0]).then_inc(out_done, 16)
            for half in range(2):
                sp.wait_ge(out_ready, 2 + half)
                ns = slice(half * NT // 2, (half + 1) * NT // 2)
                sp.dma_start(out_v[1][:, ns], out_sb[:, 1, ns]).then_inc(out_done, 16)
            sp.wait_ge(out_done, 48)

        @block.gpsimd
        def _(pool):
            nc.gpsimd.memset(ident[:], 0.0).then_inc(ident_ready, 1)
            nc.gpsimd.memset(ones[:], 1.0)
            pool.wait_ge(ident_ready, 1)
            nc.gpsimd.affine_select(out=ident[:], in_=ident[:], compare_op=ALU.not_equal, fill=1.0, base=0,
                                    pattern=[[-1, P]], channel_multiplier=1).then_inc(ident_ready, 1)
            pool.wait_ge(ident_ready, 2)
            pool.wait_ge(wbase_in, 16)
            nc.gpsimd.tensor_tensor(wbase_i[:], wbase_sb[:], ident[:], ALU.add).then_inc(wbase_i_ready, 1)

            def split_lo(s):
                for m in range(3):
                    pool.wait_ge(w_in[s][m], 16)
                    pool.wait_ge(w_hi_ready, 3 * s + m + 1)
                    nc.gpsimd.tensor_tensor(w_lo[:, s, m], w_raw[:, s, m], w_hi[:, s, m].bitcast(F32),
                                            ALU.subtract).then_inc(w_lo_ready, 1)

            split_lo(0)
            split_lo(1)
            split_lo(2)
            pool.wait_ge(bias23_in, 32)
            nc.gpsimd.tensor_scalar(bias2_b[:], ones[:], bias2[:, 0:1], 1.0, ALU.mult, ALU.mult) \
                .then_inc(bias2_b_ready, 1)
            for layer in range(2):
                for b in range(B):
                    pool.wait_ge(wsum_ready, 2 * layer + b + 1)
                    nc.gpsimd.tensor_tensor(wres[:, layer, b], wsum[:, layer, b], ident[:], ALU.add) \
                        .then_inc(wres_ready, 1)
            split_lo(3)
            split_lo(4)

        @block.scalar
        def _(act):
            act.dma_start(b_nat[:], lora_b.rearrange("e o r -> o e r")).then_inc(lora_b_in, 16)
            act.dma_start(wbase_sb[:], w_base).then_inc(wbase_in, 16)
            act.dma_start(a_sb[:], lora_a.rearrange("e r c -> (e r) c")).then_inc(lora_a_in, 16)
            act.dma_start(bias0[:], b_base.rearrange("(p a) -> p a", a=1)).then_inc(bias0_in, 16)

            act.wait_ge(topk_step, 2 * B + 1)
            nc.scalar.activation(top_exp[:], top_dif[:], ACT.Exp).then_inc(top_exp_ready, 1)
            for b in range(B):
                act.wait_ge(xT_ps_ready, b + 1)
                nc.scalar.activation(xT[:, b], xT_ps[b][:], ACT.Copy).then_inc(xT_ready, 1)
            act.wait_ge(w0_ps_ready, 1)
            nc.scalar.activation(w0_eff[:].rearrange("p b o -> p (b o)"), w0_ps[:, 0:B * P], ACT.Copy) \
                .then_inc(w0_ready, 1)
            act.wait_ge(bias0_in, 16)
            for b in range(B):
                act.wait_ge(x1_ps_ready, b + 1)
                nc.scalar.activation(x1_hi[:, b], x1_ps[b][:], ACT.Identity, bias=bias0[:, 0:1]) \
                    .then_inc(x1_hi_ready, 1)

            def w_split(s, m):
                act.wait_ge(w_in[s][m], 16)
                nc.scalar.activation(w_hi[:, s, m], w_raw[:, s, m], ACT.Copy).then_inc(w_hi_ready, 1)

            def h_upper(s):
                act.wait_ge(h_ready, s + 1)
                if s >= SLOTS:
                    act.wait_ge(down_done, s - SLOTS + 1)
                nc.scalar.activation(h_hi[:, s % SLOTS], h[:, s % SLOTS], ACT.Copy).then_inc(h_hi_ready, 1)

            split_at = {1: (1, 0), 2: (1, 1), 3: (1, 2), 4: (2, 0), 5: (2, 1), 6: (2, 2),
                        11: (3, 0), 12: (3, 1), 13: (3, 2), 14: (4, 0), 15: (4, 1), 16: (4, 2)}
            for s in range(STEPS + 1):
                if s < STEPS:
                    act.wait_ge(gate_ready, s + 1)
                    if s >= SLOTS:
                        act.wait_ge(h_ready, s - SLOTS + 1)
                    nc.scalar.activation(gelu_g[:, s % SLOTS], gate_ps[s % SLOTS][:], ACT.Gelu_apprx_tanh) \
                        .then_inc(gelu_done, 1)
                if s in split_at:
                    w_split(*split_at[s])
                if s >= 1:
                    h_upper(s - 1)
                if s == 6:
                    act.wait_ge(mask_ps_ready, 1)
                    nc.scalar.activation(maskT[:].rearrange("p l o -> p (l o)"), fold_ps[:, 0:2 * P], ACT.Copy) \
                        .then_inc(maskT_ready, 1)
                if s == 10:
                    act.wait_ge(a2_ps_ready, 1)
                    nc.scalar.activation(a2_nat[:].rearrange("p b t -> p (b t)"), fold_ps[:, 0:B * P], ACT.Copy) \
                        .then_inc(a2_ready, 1)

        @block.vector
        def _(dve):
            dve.wait_ge(condrow_in, 16)
            for b in range(B):
                nc.vector.max(top_val[:, b], cond_row[:, b]).then_inc(topk_step, 1)
            for b in range(B):
                dve.wait_ge(topk_step, b + 1)
                nc.vector.max_index(top_idx[:, b], top_val[:, b], cond_row[:, b]).then_inc(topk_step, 1)
            nc.vector.tensor_tensor(top_dif[:], top_val[:], top_val[:, :, 0:1].to_broadcast([P, B, 8]),
                                    ALU.subtract).then_inc(topk_step, 1)

            dve.wait_ge(ident_ready, 2)
            nc.vector.reduce_sum(own_group[:], ident[:].rearrange("p (a g o) -> p a g o", a=1, o=OL), AX_X) \
                .then_inc(select_step, 1)
            nc.vector.reduce_sum(delta[:], ident[:].rearrange("p (g o) -> p o g", o=OL), AX_X) \
                .then_inc(select_step, 1)
            dve.wait_ge(select_step, 1)
            nc.vector.tensor_tensor(cond_own[:], cond_row[:], own_group[:].to_broadcast([P, B, E]), ALU.mult) \
                .then_inc(select_step, 1)
            dve.wait_ge(select_step, 3)
            nc.vector.reduce_sum(cond_col[:], cond_own[:], AX_X).then_inc(select_step, 1)
            dve.wait_ge(select_step, 4)
            dve.wait_ge(bT_ps_ready, 1)
            for b in range(B):
                nc.vector.tensor_scalar(bT_w[:, b], bT_ps[:, 0:P], cond_col[:, b:b + 1], LORA_SCALING,
                                        ALU.mult, ALU.mult).then_inc(bT_w_ready, 1)
            for m in range(3):
                dve.wait_ge(w_in[0][m], 16)
                nc.vector.tensor_copy(w_hi[:, 0, m], w_raw[:, 0, m]).then_inc(w_hi_ready, 1)

            for b in range(B):
                dve.wait_ge(x1_hi_ready, b + 1)
                nc.vector.tensor_scalar(x1[:, b], x1_ps[b][:], bias0[:, 0:1], None, ALU.add).then_inc(x1_ready, 1)
                dve.wait_ge(x1_ready, b + 1)
                nc.vector.tensor_tensor(x1_lo[:, b], x1[:, b], x1_hi[:, b].bitcast(F32), ALU.subtract) \
                    .then_inc(x1_lo_ready, 1)

            done = [0]

            def route(instruction):
                done[0] += 1
                instruction.then_inc(route_step, 1)
                dve.wait_ge(route_step, done[0])

            dve.wait_ge(top_exp_ready, 1)
            route(nc.vector.reduce_sum(z_sum[:], top_exp[:], AX_X))
            route(nc.vector.reciprocal(z_inv[:], z_sum[:]))
            route(nc.vector.tensor_tensor(probs[:], top_exp[:, :, 0:2], z_inv[:].to_broadcast([P, B, 2]), ALU.mult))
            route(nc.vector.reduce_sum(pair_sum[:], probs[:], AX_X))
            route(nc.vector.reciprocal(pair_inv[:], pair_sum[:]))
            route(nc.vector.tensor_tensor(route_w[:], probs[:], pair_inv[:].to_broadcast([P, B, 2]), ALU.mult))
            assert done[0] == ROUTE_STEPS

            def h_product(s):
                b, k = UNITS[s // NC]
                i = s % SLOTS
                dve.wait_ge(up_ready, s + 1)
                dve.wait_ge(gelu_done, s + 1)
                if s >= SLOTS:
                    dve.wait_ge(h_hi_ready, s - SLOTS + 1)
                    dve.wait_ge(h_lo_ready, s - SLOTS + 1)
                if k == 0:
                    nc.vector.tensor_tensor(h[:, i], up_ps[i][:], gelu_g[:, i], ALU.mult).then_inc(h_ready, 1)
                else:
                    nc.vector.scalar_tensor_tensor(h[:, i], up_ps[i][:], route_w[:, b, k - 1:k], gelu_g[:, i],
                                                   ALU.mult, ALU.mult).then_inc(h_ready, 1)

            def h_lower(s):
                i = s % SLOTS
                dve.wait_ge(h_ready, s + 1)
                dve.wait_ge(h_hi_ready, s + 1)
                if s >= SLOTS:
                    dve.wait_ge(down_done, s - SLOTS + 1)
                nc.vector.tensor_tensor(h_lo[:, i], h[:, i], h_hi[:, i].bitcast(F32), ALU.subtract) \
                    .then_inc(h_lo_ready, 1)

            def add_bias_out(b, bank, n0, n1):
                m = n1 - n0
                nc.vector.tensor_tensor(out_sb[:, b, n0:n1], bank[:, 0:m * P].rearrange("p (n o) -> p n o", n=m),
                                        bias23[:, b:b + 1].to_broadcast([P, m, P]), ALU.add).then_inc(out_ready, 1)

            for s in range(STEPS + 1):
                if s < STEPS:
                    h_product(s)
                if s >= 1:
                    h_lower(s - 1)
                if s == 2:
                    for b in range(B):
                        nc.vector.tensor_scalar(ymat[:, b], delta[:], cond_col[:, b:b + 1], None, ALU.mult) \
                            .then_inc(ymat_ready, 1)
                if s == 8:
                    dve.wait_ge(wsum_ps_ready, 1)
                    dve.wait_ge(maskT_ready, 1)
                    for layer in range(2):
                        sums = fold_ps[:, layer * B * P:(layer + 1) * B * P].rearrange(
                            "p (oh b ol) -> p b ol oh", oh=OH, b=B)
                        for b in range(B):
                            nc.vector.tensor_tensor(
                                wsum[:, layer, b].rearrange("p (ol oh) -> p ol oh", oh=OH), sums[:, b],
                                maskT[:, layer].rearrange("p (ol oh) -> p ol oh", oh=OH), ALU.mult) \
                                .then_inc(wsum_ready, 1)
                if s == 12:
                    dve.wait_ge(w23_ps_ready, 1)
                    nc.vector.tensor_copy(w23[:].rearrange("p b o -> p (b o)"), fold_ps[:, 0:B * P]) \
                        .then_inc(w23_ready, 1)
                    dve.wait_ge(bias23_in, 32)
                    for b in range(B):
                        nc.vector.tensor_tensor(bias23[:, b], fold_ps[:, (B + b) * P:(B + b + 1) * P], bias3_b[:],
                                                ALU.add).then_inc(w23_ready, 1)
                if s == HALF + 2:
                    dve.wait_ge(down_done, HALF)
                    nc.vector.tensor_tensor(x2T[:, 0], acc_ps[0][:], x1[:, 0], ALU.add).then_inc(x2_ready, 1)
                if s == HALF + 4:
                    dve.wait_ge(out_ps_ready, 1)
                    dve.wait_ge(w23_ready, 3)
                    add_bias_out(0, acc_ps[0], 0, NT)

            dve.wait_ge(down_done, STEPS)
            for half in range(2):
                ts = slice(half * T // 2, (half + 1) * T // 2)
                nc.vector.tensor_tensor(x2T[:, 1, ts], acc_ps[1][:, ts], x1[:, 1, ts], ALU.add).then_inc(x2_ready, 1)
            for half in range(2):
                dve.wait_ge(out_ps_ready, 2 + half)
                add_bias_out(1, tail_ps[half], half * NT // 2, (half + 1) * NT // 2)

        @block.tensor
        def _(pe):
            mm = nc.tensor.matmul

            pe.wait_ge(ident_ready, 2)
            pe.wait_ge(lora_b_in, 16)
            nc.tensor.transpose(bT_ps[:, 0:P], b_nat[:].rearrange("p e r -> p (e r)"), ident[:]) \
                .then_inc(bT_ps_ready, 1)
            for b in range(B):
                pe.wait_ge(x_in[b], 16)
                for n in range(NT):
                    last = nc.tensor.transpose(xT_ps[b][:, n * P:(n + 1) * P], x_nat[:, b, n], ident[:])
                last.then_inc(xT_ps_ready, 1)
            pe.wait_ge(wbase_i_ready, 1)
            pe.wait_ge(lora_a_in, 16)
            pe.wait_ge(bT_w_ready, B)
            for b in range(B):
                o = slice(b * P, (b + 1) * P)
                mm(w0_ps[:, o], wbase_i[:], ident[:], start=True, stop=False)
                last = mm(w0_ps[:, o], a_sb[:], bT_w[:, b], start=False, stop=True)
            last.then_inc(w0_ps_ready, 1)
            pe.wait_ge(w0_ready, 1)
            for b in range(B):
                pe.wait_ge(xT_ready, b + 1)
                mm(x1_ps[b][:], w0_eff[:, b], xT[:, b], start=True, stop=True).then_inc(x1_ps_ready, 1)

            def project(ps, s, m):
                b, k = UNITS[s // NC]
                ws, c = weight_set(b, k), s % NC
                cols = slice(c * P, (c + 1) * P)
                pe.wait_ge(w_hi_ready, 3 * ws + m + 1)
                pe.wait_ge(x1_hi_ready, b + 1)
                mm(ps[:], w_hi[:, ws, m, cols], x1_hi[:, b], start=True, stop=False)
                pe.wait_ge(w_lo_ready, 3 * ws + m + 1)
                mm(ps[:], w_lo[:, ws, m, cols], x1_hi[:, b], start=False, stop=False)
                pe.wait_ge(x1_lo_ready, b + 1)
                return mm(ps[:], w_hi[:, ws, m, cols], x1_lo[:, b], start=False, stop=True)

            def gate_up(s):
                i = s % SLOTS
                if s >= SLOTS:
                    pe.wait_ge(gelu_done, s - SLOTS + 1)
                elif i == 0:
                    pe.wait_ge(xT_ready, B)
                elif i == 2:
                    pe.wait_ge(x1_ready, 1)
                project(gate_ps[i], s, 0).then_inc(gate_ready, 1)
                if s >= SLOTS:
                    pe.wait_ge(h_ready, s - SLOTS + 1)
                elif i == 2:
                    pe.wait_ge(x1_ready, 2)
                project(up_ps[i], s, 1).then_inc(up_ready, 1)

            def down(s):
                b, k = UNITS[s // NC]
                ws, c, i = weight_set(b, k), s % NC, s % SLOTS
                cols = slice(c * P, (c + 1) * P)
                first, final = s % HALF == 0, s % HALF == HALF - 1
                pe.wait_ge(w_lo_ready, 3 * ws + 3)
                pe.wait_ge(h_hi_ready, s + 1)
                mm(acc_ps[b][:], w_hi[:, ws, 2, cols], h_hi[:, i], start=first, stop=False)
                mm(acc_ps[b][:], w_lo[:, ws, 2, cols], h_hi[:, i], start=False, stop=False)
                pe.wait_ge(h_lo_ready, s + 1)
                mm(acc_ps[b][:], w_hi[:, ws, 2, cols], h_lo[:, i], start=False, stop=final).then_inc(down_done, 1)

            def output(b, bank, ns):
                for j, n in enumerate(ns):
                    last = mm(bank[:, j * P:(j + 1) * P], x2T[:, b, n * P:(n + 1) * P], w23[:, b],
                              start=True, stop=True)
                last.then_inc(out_ps_ready, 1)

            for s in range(STEPS + 2):
                if s < STEPS:
                    gate_up(s)
                if s == 5:
                    pe.wait_ge(mask_in, 32)
                    for layer in range(2):
                        last = nc.tensor.transpose(fold_ps[:, layer * P:(layer + 1) * P], mask_nat[:, layer],
                                                   ident[:])
                    last.then_inc(mask_ps_ready, 1)
                if s == 7:
                    pe.wait_ge(gw_in, 32)
                    pe.wait_ge(ymat_ready, B)
                    pe.wait_ge(maskT_ready, 1)
                    for layer in range(2):
                        for oh in range(OH):
                            o = layer * B * P + oh * B * OL
                            last = mm(fold_ps[:, o:o + B * OL], gw[:, layer, oh],
                                      ymat[:].rearrange("p b o -> p (b o)"), start=True, stop=True)
                    last.then_inc(wsum_ps_ready, 1)
                if s == 9:
                    pe.wait_ge(wsum_ready, 2 * B)
                    pe.wait_ge(wres_ready, B)
                    for b in range(B):
                        last = nc.tensor.transpose(fold_ps[:, b * P:(b + 1) * P], wres[:, 0, b], ident[:])
                    last.then_inc(a2_ps_ready, 1)
                if s == 11:
                    pe.wait_ge(a2_ready, 1)
                    pe.wait_ge(wres_ready, 2 * B)
                    pe.wait_ge(bias2_b_ready, 1)
                    for b in range(B):
                        mm(fold_ps[:, b * P:(b + 1) * P], a2_nat[:, b], wres[:, 1, b], start=True, stop=True)
                        last = mm(fold_ps[:, (B + b) * P:(B + b + 1) * P], bias2_b[:], wres[:, 1, b],
                                  start=True, stop=True)
                    last.then_inc(w23_ps_ready, 1)
                if s == HALF + 2:
                    pe.wait_ge(w23_ready, 3)
                if s >= 2:
                    down(s - 2)
                if s == HALF + 3:
                    pe.wait_ge(x2_ready, 1)
                    output(0, acc_ps[0], range(NT))
            for half in range(2):
                pe.wait_ge(x2_ready, 2 + half)
                output(1, tail_ps[half], range(half * NT // 2, (half + 1) * NT // 2))


_INS = ["x", "cond_8", "L0_cond_W_base", "L0_cond_b_base", "L0_cond_As", "L0_cond_Bs",
        "L1_cond_skill_gate", "L1_cond_skill_up", "L1_cond_skill_down",
        "L1_cond_shared_gate", "L1_cond_shared_up", "L1_cond_shared_down",
        "L2_cond_weight", "L2_cond_mask", "L2_cond_bias", "L3_cond_weight", "L3_cond_mask", "L3_cond_bias"]


def kernel(**inputs):
    import numpy as np
    import concourse.bacc as bacc
    from concourse.bass_utils import run_bass_kernel_spmd

    nc = bacc.Bacc("TRN2", target_bir_lowering=False, num_devices=1)
    arrays, args = {}, []
    for name in _INS:
        a = np.ascontiguousarray(inputs[name])
        arrays[f"in_{name}"] = a
        args.append(nc.dram_tensor(f"in_{name}", a.shape, mybir.dt.from_np(a.dtype), kind="ExternalInput").ap())
    args.append(nc.dram_tensor("out", inputs["x"].shape, F32, kind="ExternalOutput").ap())
    cond_resid_kernel(nc, *args)
    r = run_bass_kernel_spmd(nc, [arrays], core_ids=[0])
    return r.results[0]["out"]
```

```python
from contextlib import ExitStack

import concourse.bass as bass
from concourse import mybir

ALU = mybir.AluOpType
ACT = mybir.ActivationFunctionType
AX_X = mybir.AxisListType.X
F32 = mybir.dt.float32
F32R = mybir.dt.float32r
BF16 = mybir.dt.bfloat16
U32 = mybir.dt.uint32

P = 128
LORA_SCALING = 32.0 / 16


def cond_resid_kernel(
    nc: bass.Bass,
    x: bass.AP,
    cond: bass.AP,
    w_base: bass.AP,
    b_base: bass.AP,
    lora_a: bass.AP,
    lora_b: bass.AP,
    skill_gate: bass.AP,
    skill_up: bass.AP,
    skill_down: bass.AP,
    shared_gate: bass.AP,
    shared_up: bass.AP,
    shared_down: bass.AP,
    w_l2: bass.AP,
    mask_l2: bass.AP,
    bias_l2: bass.AP,
    w_l3: bass.AP,
    mask_l3: bass.AP,
    bias_l3: bass.AP,
    out: bass.AP,
):
    B, T, D = x.shape
    E = cond.shape[1]
    R = lora_a.shape[1]
    I = skill_gate.shape[2]
    assert D == P and E * R == P and T == 4 * P and B == 2
    NT = T // P
    NC = I // P

    UNITS = [(b, k) for b in range(B) for k in range(3)]
    STEPS = len(UNITS) * NC
    SLOTS = 3
    H_SLOTS = 4
    LAG = 3
    HALF = STEPS // B
    NSETS = 1 + 2 * B

    def weight_set(b, k):
        return 0 if k == 0 else 2 * b + k

    ctx = ExitStack()
    with ctx:

        def sb(name, shape, dt=F32):
            return ctx.enter_context(nc.sbuf_tensor(name, shape, dt))

        def sem(name):
            return ctx.enter_context(nc.semaphore(name))

        ident = sb("ident", [P, P])
        tiny = sb("tiny", [P, 3])
        x_nat = sb("x_nat", [P, B, NT, D])
        xT = sb("xT", [P, T])
        xT_hi = sb("xT_hi", [P, T], F32R)
        xT_lo = sb("xT_lo", [P, T], F32R)
        a_sb = sb("a_sb", [P, D])
        b_nat = sb("b_nat", [P, E, R])
        wbase_sb = sb("wbase_sb", [P, D])
        bT_w = sb("bT_w", [P, B, P])
        w0_eff = sb("w0_eff", [P, B, P])
        w0_hi = sb("w0_hi", [P, P], F32R)
        w0_lo = sb("w0_lo", [P, P], F32R)
        bias0 = sb("bias0", [P, 1])
        cond_col = sb("cond_col", [P, B])
        cond_row = sb("cond_row", [P, B, E])
        own_group = sb("own_group", [P, 1, E])
        cond_own = sb("cond_own", [P, B, E])
        top_val = sb("top_val", [P, B, 8])
        top_idx = sb("top_idx", [P, B, 8], U32)
        top_dif = sb("top_dif", [P, B, 8])
        top_exp = sb("top_exp", [P, B, 8])
        z_sum = sb("z_sum", [P, B, 1])
        z_inv = sb("z_inv", [P, B, 1])
        probs = sb("probs", [P, B, 2])
        pair_sum = sb("pair_sum", [P, B, 1])
        pair_inv = sb("pair_inv", [P, B, 1])
        route_w = sb("route_w", [P, B, 2])

        x1 = sb("x1", [P, B, T])
        x1_hi = sb("x1_hi", [P, B, T], F32R)
        x1_lo = sb("x1_lo", [P, B, T], F32R)
        w_raw = sb("w_raw", [P, NSETS, 3, I])
        w_hi = sb("w_hi", [P, NSETS, 3, I], F32R)
        w_lo = sb("w_lo", [P, NSETS, 3, I], F32R)
        gelu_g = sb("gelu_g", [P, SLOTS, T])
        h = sb("h", [P, H_SLOTS, T])
        h_hi = sb("h_hi", [P, H_SLOTS, T], F32R)
        h_lo = sb("h_lo", [P, H_SLOTS, T], F32R)

        gw = sb("gw", [P, 2, E, P])
        mask_nat = sb("mask_nat", [P, 2, P])
        wsum = sb("wsum", [P, 2, B, P])
        wmask = sb("wmask", [P, 2, B, P])
        wres = sb("wres", [P, 2, B, P])
        a3_bias = sb("a3_bias", [P, 2, B, P])
        a3T, bias23 = a3_bias[:, 0], a3_bias[:, 1]
        w23 = sb("w23", [P, B, P])
        bias2_row = sb("bias2_row", [P, P])
        bias3_col = sb("bias3_col", [P, 1])
        bias2_a3 = sb("bias2_a3", [P, B, P])
        bias2_sum = sb("bias2_sum", [P, B])
        bias23_col = sb("bias23_col", [P, B])
        x2T = sb("x2T", [P, B, T])
        out_sb = sb("out_sb", [P, B, NT, D])

        ones_bf16 = nc.const_aps.tensor(1.0, (P, P), BF16)

        def bank(name):
            return ctx.enter_context(nc.psum_tensor(name, [P, T], F32))

        gate_ps = [bank(f"gate_ps{i}") for i in range(SLOTS)]
        up_ps = [bank(f"up_ps{i}") for i in range(SLOTS)]
        acc_ps = [bank(f"acc_ps{b}") for b in range(B)]
        xT_ps = [[gate_ps[0], gate_ps[2]], [acc_ps[1], acc_ps[1]]]
        bT_ps = gate_ps[1]
        busy_ps = acc_ps[1]
        w0_ps = [up_ps[0], up_ps[1]]
        x1_ps = [[up_ps[2], acc_ps[0]], [acc_ps[1]]]
        fold_ps = acc_ps[0]
        out_ps = [[acc_ps[0], gate_ps[1]], [gate_ps[0], up_ps[0]]]

        x_in = [sem(f"x_in{b}") for b in range(B)]
        condrow_in = sem("condrow_in")
        lora_a_in = sem("lora_a_in")
        lora_b_in = sem("lora_b_in")
        wbase_in = sem("wbase_in")
        bias0_in = sem("bias0_in")
        w_in = [[sem(f"w_in{s}_{m}") for m in range(3)] for s in range(NSETS)]
        gw_in = sem("gw_in")
        mask_in = sem("mask_in")
        bias23_in = sem("bias23_in")
        out_done = sem("out_done")

        tiny_ready = sem("tiny_ready")
        ident_ready = sem("ident_ready")
        xT_ps_ready = sem("xT_ps_ready")
        xT_ready = sem("xT_ready")
        bT_ps_ready = sem("bT_ps_ready")
        bT_w_ready = sem("bT_w_ready")
        w0_ps_ready = sem("w0_ps_ready")
        w0_ready = sem("w0_ready")
        xT_hi_ready = sem("xT_hi_ready")
        xT_lo_ready = sem("xT_lo_ready")
        w0_hi_ready = sem("w0_hi_ready")
        w0_lo_ready = sem("w0_lo_ready")
        x1_ps_ready = sem("x1_ps_ready")
        x1_hi_ready = sem("x1_hi_ready")
        x1_ready = sem("x1_ready")
        x1_lo_ready = sem("x1_lo_ready")
        topk_step = sem("topk_step")
        top_exp_ready = sem("top_exp_ready")
        route_step = sem("route_step")
        w_hi_ready = sem("w_hi_ready")
        w_lo_ready = sem("w_lo_ready")
        gate_ready = sem("gate_ready")
        up_ready = sem("up_ready")
        gelu_done = sem("gelu_done")
        h_ready = sem("h_ready")
        h_hi_ready = sem("h_hi_ready")
        h_lo_by_dve = sem("h_lo_by_dve")
        h_lo_by_pool = sem("h_lo_by_pool")
        down_done = sem("down_done")
        select_step = sem("select_step")
        wsum_step = sem("wsum_step")
        wmask_ready = sem("wmask_ready")
        wres_ready = sem("wres_ready")
        bias2_a3_ready = sem("bias2_a3_ready")
        bias_step = sem("bias_step")
        a3_ps_ready = sem("a3_ps_ready")
        a3_ready = sem("a3_ready")
        w23_ps_ready = sem("w23_ps_ready")
        w23_ready = sem("w23_ready")
        x2_ready = sem("x2_ready")
        out_ps_ready = sem("out_ps_ready")
        out_ready = sem("out_ready")

        SPLIT_AT = {3 * n + m: (ws, m) for n, ws in enumerate(range(1, NSETS)) for m in range(3)}
        ROW1_AT = 8
        FOLD_AT = 20
        SUMS_AT = {s: 2 for s in range(3, 13)} | {s: 3 for s in range(13, 17)}
        POOL_LO = (13, 15)

        def h_lo_made(s):
            if s in POOL_LO:
                return h_lo_by_pool, POOL_LO.index(s) + 1
            return h_lo_by_dve, s + 1 - sum(n < s for n in POOL_LO)

        def h_columns(s):
            return [slice(0, T // 2), slice(T // 2, T)] if s == STEPS - 1 else [slice(0, T)]

        def x1_columns(b, half):
            n = T // len(x1_ps[b])
            return slice(half * n, (half + 1) * n)

        TAIL_ORDER = (1, 0)
        BUSY_AT_START, BUSY_BEFORE_LAYER0 = 24 * P, 4 * P

        CHAINS = 2 * B

        block = ctx.enter_context(nc.Block())

        @block.sync
        def _(sp):
            x_v = x.rearrange("b (p n) d -> b p n d", n=NT)
            sp.dma_start(b_nat[:], lora_b.rearrange("e o r -> o e r")).then_inc(lora_b_in, 16)
            sp.dma_start(x_nat[:, 0], x_v[0]).then_inc(x_in[0], 16)
            sp.dma_start(a_sb[:], lora_a.rearrange("e r c -> (e r) c")).then_inc(lora_a_in, 16)
            sp.dma_start(w_raw[:, 0, 0], shared_gate).then_inc(w_in[0][0], 16)
            sp.dma_start(x_nat[:, 1], x_v[1]).then_inc(x_in[1], 16)
            sp.dma_start(bias0[:], b_base.rearrange("(p a) -> p a", a=1)).then_inc(bias0_in, 16)
            sp.dma_start(w_raw[:, 0, 1], shared_up).then_inc(w_in[0][1], 16)
            sp.dma_start(w_raw[:, 0, 2].rearrange("p (c d) -> p c d", c=NC),
                         shared_down.rearrange("(c p) d -> p c d", p=P)).then_inc(w_in[0][2], 16)

            def fetch_experts(b):
                for k in range(2):
                    e = sp.value_load(top_idx[0:1, b, k:k + 1], min_val=0, max_val=E - 1)
                    s = weight_set(b, k + 1)
                    sp.dma_start(w_raw[:, s, 0], skill_gate[bass.ds(e, 1)].rearrange("a h i -> (a h) i")) \
                        .then_inc(w_in[s][0], 16)
                    sp.dma_start(w_raw[:, s, 1], skill_up[bass.ds(e, 1)].rearrange("a h i -> (a h) i")) \
                        .then_inc(w_in[s][1], 16)
                    sp.dma_start(w_raw[:, s, 2].rearrange("p (c d) -> p c d", c=NC),
                                 skill_down[bass.ds(e, 1)].rearrange("a (c p) d -> p (a c) d", p=P)) \
                        .then_inc(w_in[s][2], 16)

            sp.wait_ge(topk_step, 2 * B + 1)
            fetch_experts(0)
            for layer, (w, m) in enumerate([(w_l2, mask_l2), (w_l3, mask_l3)]):
                sp.dma_start(mask_nat[:, layer], m).then_inc(mask_in, 16)
                sp.dma_start(gw[:, layer], w.rearrange("g o t -> o g t")).then_inc(gw_in, 16)
            sp.dma_start(bias2_row[:], bias_l2.partition_broadcast(P)).then_inc(bias23_in, 16)
            sp.dma_start(bias3_col[:], bias_l3.rearrange("(p a) -> p a", a=1)).then_inc(bias23_in, 16)
            fetch_experts(1)

            out_v = out.rearrange("b (p n) d -> b p n d", n=NT)
            first, second = slice(0, NT // 2), slice(NT // 2, NT)
            sp.wait_ge(out_ready, 1)
            sp.dma_start(out_v[0][:, first], out_sb[:, 0, first]).then_inc(out_done, 16)
            sp.wait_ge(out_ready, 3)
            sp.dma_start(out.rearrange("b (p n) d -> p b n d", n=NT)[:, :, second], out_sb[:, :, second]) \
                .then_inc(out_done, 16)
            sp.wait_ge(out_ready, 4)
            sp.dma_start(out_v[1][:, first], out_sb[:, 1, first]).then_inc(out_done, 16)
            sp.wait_ge(out_done, 3 * 16)

        @block.gpsimd
        def _(pool):
            pool.dma_start(wbase_sb[:], w_base).then_inc(wbase_in, 16)
            nc.gpsimd.memset(tiny[:], 0.0).then_inc(tiny_ready, 1)
            nc.gpsimd.memset(ident[:], 0.0).then_inc(ident_ready, 1)
            pool.wait_ge(ident_ready, 1)
            nc.gpsimd.affine_select(out=ident[:], in_=ident[:], compare_op=ALU.not_equal, fill=1.0, base=0,
                                    pattern=[[-1, P]], channel_multiplier=1).then_inc(ident_ready, 1)

            def split_lo(ws, m):
                pool.wait_ge(w_in[ws][m], 16)
                pool.wait_ge(w_hi_ready, 3 * ws + m + 1)
                nc.gpsimd.tensor_tensor(w_lo[:, ws, m], w_raw[:, ws, m], w_hi[:, ws, m].bitcast(F32),
                                        ALU.subtract).then_inc(w_lo_ready, 1)

            for m in range(3):
                split_lo(0, m)
            pool.wait_ge(w0_ready, 2)
            pool.wait_ge(w0_hi_ready, 1)
            nc.gpsimd.tensor_tensor(w0_lo[:], w0_eff[:, 1], w0_hi[:].bitcast(F32), ALU.subtract) \
                .then_inc(w0_lo_ready, 1)
            for s in range(STEPS):
                if s in SPLIT_AT:
                    split_lo(*SPLIT_AT[s])
                if s in POOL_LO:
                    i = s % H_SLOTS
                    pool.wait_ge(h_ready, s + 1)
                    pool.wait_ge(h_hi_ready, s + 1)
                    pool.wait_ge(down_done, s - H_SLOTS + 1)
                    nc.gpsimd.tensor_tensor(h_lo[:, i], h[:, i], h_hi[:, i].bitcast(F32), ALU.subtract) \
                        .then_inc(h_lo_by_pool, 1)
            pool.wait_ge(wsum_step, CHAINS * E)
            pool.wait_ge(ident_ready, 2)
            pool.wait_ge(mask_in, 32)
            for n, layer in enumerate((1, 0)):
                for b in range(B):
                    nc.gpsimd.tensor_tensor(wmask[:, layer, b], wsum[:, layer, b], mask_nat[:, layer], ALU.mult) \
                        .then_inc(wmask_ready, 1)
                for b in range(B):
                    pool.wait_ge(wmask_ready, B * n + b + 1)
                    nc.gpsimd.tensor_tensor(wres[:, layer, b], wmask[:, layer, b], ident[:], ALU.add) \
                        .then_inc(wres_ready, 1)
                if layer == 1:
                    pool.wait_ge(bias23_in, 32)
                    for b in range(B):
                        pool.wait_ge(wres_ready, b + 1)
                        nc.gpsimd.tensor_tensor(bias2_a3[:, b], wres[:, 1, b], bias2_row[:], ALU.mult) \
                            .then_inc(bias2_a3_ready, 1)

        @block.scalar
        def _(act):
            act.dma_start(cond_row[:].rearrange("p b e -> p (b e)"),
                          cond.rearrange("b e -> (b e)").partition_broadcast(P)).then_inc(condrow_in, 16)

            act.wait_ge(tiny_ready, 1)
            nc.scalar.activation(tiny[:, 1:2], tiny[:, 0:1], ACT.Exp)

            act.wait_ge(topk_step, B + 1)
            nc.scalar.activation(top_exp[:], top_dif[:], ACT.Exp).then_inc(top_exp_ready, 1)
            nc.scalar.activation(tiny[:, 2:3], tiny[:, 0:1], ACT.Gelu_apprx_tanh)

            def w_split(s, m):
                act.wait_ge(w_in[s][m], 16)
                nc.scalar.activation(w_hi[:, s, m], w_raw[:, s, m], ACT.Copy).then_inc(w_hi_ready, 1)

            def x1_upper(b):
                act.wait_ge(bias0_in, 16)
                for half, bank in enumerate(x1_ps[b]):
                    ts = x1_columns(b, half)
                    act.wait_ge(x1_ps_ready, 2 * b + half + 1)
                    nc.scalar.activation(x1_hi[:, b, ts], bank[:, 0:ts.stop - ts.start], ACT.Identity,
                                         bias=bias0[:, 0:1]).then_inc(x1_hi_ready, 1)

            x1_upper(0)
            act.wait_ge(xT_ps_ready, 3)
            nc.scalar.activation(xT_hi[:], xT_ps[1][0][:], ACT.Copy).then_inc(xT_hi_ready, 1)
            act.wait_ge(w_hi_ready, 2)
            w_split(0, 2)
            act.wait_ge(w0_ready, 2)
            nc.scalar.activation(w0_hi[:], w0_eff[:, 1], ACT.Copy).then_inc(w0_hi_ready, 1)

            def h_upper(s):
                if s >= H_SLOTS:
                    act.wait_ge(down_done, s - H_SLOTS + 1)
                for part, ts in enumerate(h_columns(s)):
                    act.wait_ge(h_ready, s + part + 1)
                    nc.scalar.activation(h_hi[:, s % H_SLOTS, ts], h[:, s % H_SLOTS, ts], ACT.Copy) \
                        .then_inc(h_hi_ready, 1)

            for s in range(STEPS + 1):
                if s < STEPS:
                    act.wait_ge(gate_ready, s + 1)
                    if s >= SLOTS:
                        act.wait_ge(h_ready, s - SLOTS + 1)
                    nc.scalar.activation(gelu_g[:, s % SLOTS], gate_ps[s % SLOTS][:], ACT.Gelu_apprx_tanh) \
                        .then_inc(gelu_done, 1)
                if s >= 1:
                    h_upper(s - 1)
                if s in SPLIT_AT:
                    w_split(*SPLIT_AT[s])
                if s == ROW1_AT + 1:
                    x1_upper(1)
                if s == FOLD_AT + 1:
                    act.wait_ge(a3_ps_ready, 1)
                    nc.scalar.activation(a3_bias[:].rearrange("p a b t -> p (a b t)"), fold_ps[:], ACT.Copy) \
                        .then_inc(a3_ready, 1)

        @block.vector
        def _(dve):
            dve.wait_ge(ident_ready, 2)
            nc.vector.reduce_sum(own_group[:], ident[:].rearrange("p (a g o) -> p a g o", a=1, o=R), AX_X) \
                .then_inc(select_step, 1)
            dve.wait_ge(condrow_in, 16)
            dve.wait_ge(select_step, 1)
            nc.vector.tensor_tensor(cond_own[:], cond_row[:], own_group[:].to_broadcast([P, B, E]), ALU.mult) \
                .then_inc(select_step, 1)
            nc.vector.max(top_val[:, 0], cond_row[:, 0]).then_inc(topk_step, 1)
            dve.wait_ge(select_step, 2)
            nc.vector.reduce_sum(cond_col[:], cond_own[:], AX_X).then_inc(select_step, 1)
            nc.vector.max(top_val[:, 1], cond_row[:, 1]).then_inc(topk_step, 1)

            def weight_lora(b):
                nc.vector.tensor_scalar(bT_w[:, b], bT_ps[:, 0:P], cond_col[:, b:b + 1], LORA_SCALING,
                                        ALU.mult, ALU.mult).then_inc(bT_w_ready, 1)

            dve.wait_ge(select_step, 3)
            dve.wait_ge(bT_ps_ready, 1)
            for b in range(B):
                weight_lora(b)
            dve.wait_ge(topk_step, B)
            nc.vector.tensor_tensor(top_dif[:], top_val[:], top_val[:, :, 0:1].to_broadcast([P, B, 8]),
                                    ALU.subtract).then_inc(topk_step, 1)
            for b in range(B):
                nc.vector.max_index(top_idx[:, b], top_val[:, b], cond_row[:, b]).then_inc(topk_step, 1)

            def copy_xT(half):
                ts = slice(half * T // 2, (half + 1) * T // 2)
                dve.wait_ge(xT_ps_ready, half + 1)
                nc.vector.tensor_copy(xT[:, ts], xT_ps[0][half][:, ts]).then_inc(xT_ready, 1)

            def layer0_weight(b):
                dve.wait_ge(w0_ps_ready, b + 1)
                nc.vector.tensor_tensor(w0_eff[:, b], w0_ps[b][:, 0:P], ident[:], ALU.add).then_inc(w0_ready, 1)

            copy_xT(0)
            layer0_weight(0)
            copy_xT(1)
            layer0_weight(1)

            for m in range(2):
                dve.wait_ge(w_in[0][m], 16)
                nc.vector.tensor_copy(w_hi[:, 0, m], w_raw[:, 0, m]).then_inc(w_hi_ready, 1)

            def x1_lower(b):
                for half, bank in enumerate(x1_ps[b]):
                    ts = x1_columns(b, half)
                    dve.wait_ge(x1_hi_ready, 2 * b + half + 1)
                    nc.vector.tensor_scalar(x1[:, b, ts], bank[:, 0:ts.stop - ts.start], bias0[:, 0:1], None,
                                            ALU.add).then_inc(x1_ready, 1)
                dve.wait_ge(x1_ready, 2 + b)
                nc.vector.tensor_tensor(x1_lo[:, b], x1[:, b], x1_hi[:, b].bitcast(F32), ALU.subtract) \
                    .then_inc(x1_lo_ready, 1)

            dve.wait_ge(bias0_in, 16)
            x1_lower(0)
            dve.wait_ge(xT_ps_ready, 3)
            dve.wait_ge(xT_hi_ready, 1)
            nc.vector.tensor_tensor(xT_lo[:], xT_ps[1][0][:], xT_hi[:].bitcast(F32), ALU.subtract) \
                .then_inc(xT_lo_ready, 1)

            def routing_weights():
                done = [0]

                def route(instruction):
                    done[0] += 1
                    instruction.then_inc(route_step, 1)
                    dve.wait_ge(route_step, done[0])

                dve.wait_ge(top_exp_ready, 1)
                route(nc.vector.reduce_sum(z_sum[:], top_exp[:], AX_X))
                route(nc.vector.reciprocal(z_inv[:], z_sum[:]))
                route(nc.vector.tensor_tensor(probs[:], top_exp[:, :, 0:2], z_inv[:].to_broadcast([P, B, 2]), ALU.mult))
                route(nc.vector.reduce_sum(pair_sum[:], probs[:], AX_X))
                route(nc.vector.reciprocal(pair_inv[:], pair_sum[:]))
                route(nc.vector.tensor_tensor(route_w[:], probs[:], pair_inv[:].to_broadcast([P, B, 2]), ALU.mult))

            assert sum(SUMS_AT.values()) == CHAINS * E

            def group_sums(first, count):
                for n in range(first, first + count):
                    g, layer, b = n // CHAINS, n % CHAINS // B, n % B
                    scalar = cond_row[:, b, g:g + 1]
                    dve.wait_ge(gw_in, 32)
                    if g == 0:
                        nc.vector.tensor_scalar(wsum[:, layer, b], gw[:, layer, g], scalar, None, ALU.mult) \
                            .then_inc(wsum_step, 1)
                    else:
                        dve.wait_ge(wsum_step, n - CHAINS + 1)
                        nc.vector.scalar_tensor_tensor(wsum[:, layer, b], gw[:, layer, g], scalar, wsum[:, layer, b],
                                                       ALU.mult, ALU.add).then_inc(wsum_step, 1)

            def h_product(s):
                b, k = UNITS[s // NC]
                i, j = s % SLOTS, s % H_SLOTS
                dve.wait_ge(up_ready, s + 1)
                dve.wait_ge(gelu_done, s + 1)
                if s >= H_SLOTS:
                    dve.wait_ge(h_hi_ready, s - H_SLOTS + 1)
                    dve.wait_ge(*h_lo_made(s - H_SLOTS))
                for ts in h_columns(s):
                    if k == 0:
                        nc.vector.tensor_tensor(h[:, j, ts], up_ps[i][:, ts], gelu_g[:, i, ts], ALU.mult) \
                            .then_inc(h_ready, 1)
                    else:
                        nc.vector.scalar_tensor_tensor(h[:, j, ts], up_ps[i][:, ts], route_w[:, b, k - 1:k],
                                                       gelu_g[:, i, ts], ALU.mult, ALU.mult).then_inc(h_ready, 1)

            def h_lower(s):
                i = s % H_SLOTS
                dve.wait_ge(h_ready, s + len(h_columns(s)))
                dve.wait_ge(h_hi_ready, s + len(h_columns(s)))
                if s >= H_SLOTS:
                    dve.wait_ge(down_done, s - H_SLOTS + 1)
                nc.vector.tensor_tensor(h_lo[:, i], h[:, i], h_hi[:, i].bitcast(F32), ALU.subtract) \
                    .then_inc(h_lo_by_dve, 1)

            def output(b, half):
                m = NT // 2
                dve.wait_ge(out_ps_ready, 2 * b + (half if b == 0 else TAIL_ORDER.index(half)) + 1)
                nc.vector.tensor_tensor(out_sb[:, b, half * m:(half + 1) * m],
                                        out_ps[b][half][:, 0:m * P].rearrange("p (n o) -> p n o", n=m),
                                        bias23[:, b:b + 1].to_broadcast([P, m, P]), ALU.add).then_inc(out_ready, 1)

            for s in range(STEPS + 1):
                if s < STEPS:
                    h_product(s)
                if s >= 1 and s - 1 not in POOL_LO:
                    h_lower(s - 1)
                if s == 2:
                    routing_weights()
                if s == ROW1_AT + 1:
                    x1_lower(1)
                if s in SUMS_AT:
                    group_sums(sum(n for t, n in SUMS_AT.items() if t < s), SUMS_AT[s])
                if s == HALF + 3:
                    dve.wait_ge(down_done, HALF)
                    nc.vector.tensor_tensor(x2T[:, 0], acc_ps[0][:], x1[:, 0], ALU.add).then_inc(x2_ready, 1)
                if s == FOLD_AT - 2:
                    dve.wait_ge(bias2_a3_ready, B)
                    nc.vector.reduce_sum(bias2_sum[:], bias2_a3[:], AX_X).then_inc(bias_step, 1)
                    dve.wait_ge(bias_step, 1)
                    nc.vector.tensor_scalar(bias23_col[:], bias2_sum[:], bias3_col[:, 0:1], None, ALU.add) \
                        .then_inc(bias_step, 1)
                if s == FOLD_AT + 2:
                    dve.wait_ge(w23_ps_ready, 1)
                    nc.vector.tensor_copy(w23[:].rearrange("p b o -> p (b o)"), fold_ps[:, 0:B * P]) \
                        .then_inc(w23_ready, 1)
            dve.wait_ge(a3_ready, 1)
            output(0, 0)
            dve.wait_ge(down_done, STEPS)
            for half in TAIL_ORDER:
                for n in range(half * NT // 2, (half + 1) * NT // 2):
                    ts = slice(n * P, (n + 1) * P)
                    nc.vector.tensor_tensor(x2T[:, 1, ts], acc_ps[1][:, ts], x1[:, 1, ts], ALU.add) \
                        .then_inc(x2_ready, 1)
            output(0, 1)
            for half in TAIL_ORDER:
                output(1, half)

        @block.tensor
        def _(pe):
            mm = nc.tensor.matmul

            def keep_busy(columns):
                for first in range(0, columns, P):
                    n = min(P, columns - first)
                    mm(busy_ps[:, 0:n], ones_bf16, ones_bf16[:, 0:n], start=True, stop=True)

            def transpose_x(b, ns):
                pe.wait_ge(x_in[b], 16)
                for n in ns:
                    last = nc.tensor.transpose(xT_ps[b][2 * n // NT][:, n * P:(n + 1) * P], x_nat[:, b, n], ident[:])
                last.then_inc(xT_ps_ready, 1)

            def layer0_base(b):
                pe.wait_ge(wbase_in, 16)
                mm(w0_ps[b][:, 0:P], wbase_sb[:], ident[:], start=True, stop=False)

            def layer0_lora(b):
                pe.wait_ge(bT_w_ready, b + 1)
                pe.wait_ge(lora_a_in, 16)
                mm(w0_ps[b][:, 0:P], a_sb[:], bT_w[:, b], start=False, stop=True).then_inc(w0_ps_ready, 1)

            def layer0_row0():
                pe.wait_ge(w0_ready, 1)
                for half, bank in enumerate(x1_ps[0]):
                    ts = x1_columns(0, half)
                    pe.wait_ge(xT_ready, half + 1)
                    mm(bank[:, 0:ts.stop - ts.start], w0_eff[:, 0], xT[:, ts], start=True, stop=True) \
                        .then_inc(x1_ps_ready, 1)

            def layer0_row1():
                bank = x1_ps[1][0]
                pe.wait_ge(xT_hi_ready, 1)
                pe.wait_ge(w0_hi_ready, 1)
                pe.wait_ge(w0_lo_ready, 1)
                pe.wait_ge(xT_lo_ready, 1)
                mm(bank[:], w0_hi[:], xT_hi[:], start=True, stop=False)
                mm(bank[:], w0_lo[:], xT_hi[:], start=False, stop=False)
                mm(bank[:], w0_hi[:], xT_lo[:], start=False, stop=True).then_inc(x1_ps_ready, 1)

            keep_busy(BUSY_AT_START)
            pe.wait_ge(ident_ready, 2)
            pe.wait_ge(lora_b_in, 16)
            nc.tensor.transpose(bT_ps[:, 0:P], b_nat[:].rearrange("p e r -> p (e r)"), ident[:]) \
                .then_inc(bT_ps_ready, 1)
            for b in range(B):
                layer0_base(b)
            transpose_x(0, range(0, NT // 2))
            layer0_lora(0)
            transpose_x(0, range(NT // 2, NT))
            layer0_lora(1)
            keep_busy(BUSY_BEFORE_LAYER0)
            layer0_row0()
            transpose_x(1, range(NT))

            def product(s, m, part):
                b, k = UNITS[s // NC]
                ws, c = weight_set(b, k), s % NC
                cols = slice(c * P, (c + 1) * P)
                ps = (gate_ps, up_ps)[m][s % SLOTS]
                if part == 0:
                    if s >= SLOTS:
                        pe.wait_ge((gelu_done, h_ready)[m], s - SLOTS + 1)
                    pe.wait_ge(w_hi_ready, 3 * ws + m + 1)
                    pe.wait_ge(x1_hi_ready, b + 2)
                    mm(ps[:], w_hi[:, ws, m, cols], x1_hi[:, b], start=True, stop=False)
                elif part == 1:
                    pe.wait_ge(w_lo_ready, 3 * ws + m + 1)
                    mm(ps[:], w_lo[:, ws, m, cols], x1_hi[:, b], start=False, stop=False)
                else:
                    pe.wait_ge(x1_lo_ready, b + 1)
                    mm(ps[:], w_hi[:, ws, m, cols], x1_lo[:, b], start=False, stop=True) \
                        .then_inc((gate_ready, up_ready)[m], 1)

            def down_upper(s):
                b, k = UNITS[s // NC]
                ws, c, i = weight_set(b, k), s % NC, s % H_SLOTS
                cols = slice(c * P, (c + 1) * P)
                pe.wait_ge(w_lo_ready, 3 * ws + 3)
                pe.wait_ge(h_hi_ready, s + len(h_columns(s)))
                mm(acc_ps[b][:], w_hi[:, ws, 2, cols], h_hi[:, i], start=s % HALF == 0, stop=False)
                mm(acc_ps[b][:], w_lo[:, ws, 2, cols], h_hi[:, i], start=False, stop=False)

            def down_lower(s):
                b, k = UNITS[s // NC]
                ws, c, i = weight_set(b, k), s % NC, s % H_SLOTS
                cols = slice(c * P, (c + 1) * P)
                pe.wait_ge(*h_lo_made(s))
                mm(acc_ps[b][:], w_hi[:, ws, 2, cols], h_lo[:, i], start=False, stop=s % HALF == HALF - 1) \
                    .then_inc(down_done, 1)

            def output(b, half):
                for j in range(NT // 2):
                    if b == 1:
                        pe.wait_ge(x2_ready, 2 + TAIL_ORDER.index(half) * NT // 2 + j)
                    n = half * NT // 2 + j
                    last = mm(out_ps[b][half][:, j * P:(j + 1) * P], x2T[:, b, n * P:(n + 1) * P], w23[:, b],
                              start=True, stop=True)
                last.then_inc(out_ps_ready, 1)

            pe.wait_ge(w0_ready, B)
            pe.wait_ge(w_hi_ready, 1)
            for half in range(2):
                ts = x1_columns(0, half)
                pe.wait_ge(x1_hi_ready, half + 1)
                for s in range(SLOTS):
                    mm(gate_ps[s][:, ts], w_hi[:, 0, 0, s * P:(s + 1) * P], x1_hi[:, 0, ts],
                       start=half == 0, stop=False)
            for s in range(SLOTS):
                if s == SLOTS - 1:
                    pe.wait_ge(x1_ready, 1)
                product(s, 1, 0)
            for s in range(SLOTS):
                product(s, 0, 1)
            for s in range(SLOTS):
                product(s, 0, 2)
                product(s, 1, 1)
                product(s, 1, 2)
            pe.wait_ge(x1_ready, 2)
            for s in range(SLOTS, STEPS + LAG):
                if s < STEPS:
                    for m in range(2):
                        for part in range(3):
                            product(s, m, part)
                if s == ROW1_AT:
                    layer0_row1()
                if s == FOLD_AT:
                    pe.wait_ge(x2_ready, 1)
                    pe.wait_ge(wres_ready, B)
                    for b in range(B):
                        nc.tensor.transpose(fold_ps[:, b * P:(b + 1) * P], wres[:, 1, b], ident[:])
                    pe.wait_ge(bias_step, 2)
                    for b in range(B):
                        last = nc.tensor.transpose(fold_ps[:, (B + b) * P:(B + b + 1) * P],
                                                   bias23_col[:, b:b + 1].to_broadcast([P, P]), ident[:])
                    last.then_inc(a3_ps_ready, 1)
                if s == FOLD_AT + 2:
                    pe.wait_ge(a3_ready, 1)
                    pe.wait_ge(wres_ready, 2 * B)
                    for b in range(B):
                        last = mm(fold_ps[:, b * P:(b + 1) * P], wres[:, 0, b], a3T[:, b], start=True, stop=True)
                    last.then_inc(w23_ps_ready, 1)
                if s == HALF + LAG:
                    pe.wait_ge(x1_ready, 3)
                down_upper(s - LAG)
                if s == STEPS + LAG - 2:
                    pe.wait_ge(w23_ready, 1)
                    output(0, 0)
                down_lower(s - LAG)
            output(0, 1)
            for half in TAIL_ORDER:
                output(1, half)


_INS = ["x", "cond_8", "L0_cond_W_base", "L0_cond_b_base", "L0_cond_As", "L0_cond_Bs",
        "L1_cond_skill_gate", "L1_cond_skill_up", "L1_cond_skill_down",
        "L1_cond_shared_gate", "L1_cond_shared_up", "L1_cond_shared_down",
        "L2_cond_weight", "L2_cond_mask", "L2_cond_bias", "L3_cond_weight", "L3_cond_mask", "L3_cond_bias"]


def kernel(**inputs):
    import numpy as np
    import concourse.bacc as bacc
    from concourse.bass_utils import run_bass_kernel_spmd

    nc = bacc.Bacc("TRN2", target_bir_lowering=False, num_devices=1)
    arrays, args = {}, []
    for name in _INS:
        a = np.ascontiguousarray(inputs[name])
        arrays[f"in_{name}"] = a
        args.append(nc.dram_tensor(f"in_{name}", a.shape, mybir.dt.from_np(a.dtype), kind="ExternalInput").ap())
    args.append(nc.dram_tensor("out", inputs["x"].shape, F32, kind="ExternalOutput").ap())
    cond_resid_kernel(nc, *args)
    r = run_bass_kernel_spmd(nc, [arrays], core_ids=[0])
    return r.results[0]["out"]
```
